# Optimizing a Trainium2 kernel written in Bass

```python
import numpy as np
import jax
import jax.numpy as jnp

def _softmax(x, axis=-1):
    return jax.nn.softmax(x, axis=axis)

def _gelu(x):
    return jax.nn.gelu(x, approximate=True)

def _silu(x):
    return jax.nn.silu(x)

def _sigmoid(x):
    return jax.nn.sigmoid(x)

def _layernorm(x, axis=-1, eps=1e-05):
    m = jnp.mean(x, axis=axis, keepdims=True)
    v = jnp.var(x, axis=axis, keepdims=True)
    return (x - m) / jnp.sqrt(v + eps)

def _scatter_add(tgt, idx, src, axis=0):
    return tgt.at[idx].add(src)

def _segment_sum(src, seg, n):
    return jax.ops.segment_sum(src, seg, n)
kernel_name = 'mk_xattn_ffn_d1_seqx_r8_0d5e2b'

def setup_inputs(seed: int=0):
    np.random.seed(seed)
    _w = jnp.asarray

    def _rec_inputs():
        import jax
        import jax.numpy as jnp
        _rk = jax.random.key(seed)
        x = -7.109e-05 + 0.9999 * jax.random.normal(jax.random.fold_in(_rk, 1), (4, 256, 256), jnp.float32)
        _lenS = 256 - jax.random.randint(jax.random.fold_in(_rk, 7), (4,), 0, max(1, 256 // 4) + 1, jnp.int32)
        _lenS2 = 256 - jax.random.randint(jax.random.fold_in(_rk, 8), (4,), 0, max(1, 256 // 4) + 1, jnp.int32)
        _ctx_512P = jax.random.normal(jax.random.fold_in(_rk, 11), (4, 16, 64), jnp.float32)
        _ctx_512c = jax.random.dirichlet(jax.random.fold_in(_rk, 511), 0.3 * jnp.ones((16,), jnp.float32), (4, 256))
        _ctx_512t = jnp.einsum('bsk,bkd->bsd', _ctx_512c, _ctx_512P)
        _ctx_512t = _ctx_512t * jax.lax.rsqrt(jnp.mean(jnp.square(_ctx_512t)) + 1e-12) * 0.953939
        ctx_512 = 2.81802e-05 + 1.00001 * (_ctx_512t + 0.3 * jax.random.normal(jax.random.fold_in(_rk, 611), (4, 256, 64), jnp.float32))
        return (x, ctx_512)
    x, ctx_512 = _rec_inputs()

    def _L0_xattn_setup():
        import jax, jax.numpy as jnp
        import numpy as np
        EPS = 1e-06
        IMAGE_DIMS = 256
        key = jax.random.key(seed)
        k1, k2, k3 = jax.random.split(key, 3)
        B, I, J, D = (16, 256, 256, 64)
        p = jax.random.normal(k1, (B, I, J), dtype=jnp.float32)
        k_v = jax.random.normal(k2, (B, J, D), dtype=jnp.float32)
        W_k = jax.random.normal(k3, (D, D), dtype=jnp.float32) * (1.0 / np.sqrt(D))
        b_k = jnp.zeros((D,), dtype=jnp.float32)
        ln_gamma = jnp.ones((J,), dtype=jnp.float32)
        ln_beta = jnp.zeros((J,), dtype=jnp.float32)
        return {'p': p, 'k_v': k_v, 'W_k': W_k, 'b_k': b_k, 'ln_gamma': ln_gamma, 'ln_beta': ln_beta}
    _L0_xattn_all = _L0_xattn_setup()
    _L0_xattn_in = {k: v for k, v in _L0_xattn_all.items() if k in ('W_k', 'b_k', 'ln_gamma', 'ln_beta')}
    del _L0_xattn_all

    def _L0_ffn_setup():
        import jax, jax.numpy as jnp
        import numpy as np
        B, S, H = (1, 64, 256)
        I = 192
        E = 32
        K = 4
        SCALE = 1.8
        key = jax.random.key(seed)
        ks = jax.random.split(key, 9)
        init = lambda k, shape: jax.random.normal(k, shape, jnp.float32) * (1.0 / np.sqrt(shape[-1]))
        return {'x': jax.random.normal(ks[0], (B, S, H), jnp.float32), 'router_w': init(ks[1], (E, H)), 'router_b': jnp.zeros((E,), jnp.float32), 'gate_w': init(ks[2], (E, I, H)), 'up_w': init(ks[3], (E, I, H)), 'down_w': init(ks[4], (E, H, I)), 'shared_gate_w': init(ks[5], (I, H)), 'shared_up_w': init(ks[6], (I, H)), 'shared_down_w': init(ks[7], (H, I))}
    _L0_ffn_all = _L0_ffn_setup()
    _L0_ffn_in = {k: v for k, v in _L0_ffn_all.items() if k in ('router_w', 'router_b', 'gate_w', 'up_w', 'down_w', 'shared_gate_w', 'shared_up_w', 'shared_down_w')}
    del _L0_ffn_all
    return {'x': x, 'ctx_512': ctx_512, 'L0_xattn_W_k': _L0_xattn_in['W_k'], 'L0_xattn_b_k': _L0_xattn_in['b_k'], 'L0_xattn_ln_gamma': _L0_xattn_in['ln_gamma'], 'L0_xattn_ln_beta': _L0_xattn_in['ln_beta'], 'L0_ffn_router_w': _L0_ffn_in['router_w'], 'L0_ffn_router_b': _L0_ffn_in['router_b'], 'L0_ffn_gate_w': _L0_ffn_in['gate_w'], 'L0_ffn_up_w': _L0_ffn_in['up_w'], 'L0_ffn_down_w': _L0_ffn_in['down_w'], 'L0_ffn_shared_gate_w': _L0_ffn_in['shared_gate_w'], 'L0_ffn_shared_up_w': _L0_ffn_in['shared_up_w'], 'L0_ffn_shared_down_w': _L0_ffn_in['shared_down_w']}

def reference(x, ctx_512, L0_xattn_W_k, L0_xattn_b_k, L0_xattn_ln_gamma, L0_xattn_ln_beta, L0_ffn_router_w, L0_ffn_router_b, L0_ffn_gate_w, L0_ffn_up_w, L0_ffn_down_w, L0_ffn_shared_gate_w, L0_ffn_shared_up_w, L0_ffn_shared_down_w):
    import jax
    import jax.numpy as jnp

    def _L0_xattn_ref(p, k_v, W_k, b_k, ln_gamma, ln_beta):
        import jax, jax.numpy as jnp
        import numpy as np
        EPS = 1e-06
        IMAGE_DIMS = 256
        kv = k_v @ W_k.T + b_k
        out = jnp.einsum('bij,bjd->bid', p, kv)
        scale = IMAGE_DIMS ** (-0.5)
        sim = jnp.einsum('bid,bjd->bij', out, kv) * scale
        mu = jnp.mean(sim, axis=-1, keepdims=True)
        var = jnp.var(sim, axis=-1, keepdims=True)
        sim = (sim - mu) * jax.lax.rsqrt(var + EPS) * ln_gamma + ln_beta
        attn = jax.nn.softmax(sim, axis=-1)
        return attn

    def _L0_ffn_ref(x, router_w, router_b, gate_w, up_w, down_w, shared_gate_w, shared_up_w, shared_down_w):
        import jax, jax.numpy as jnp
        import numpy as np
        B, S, H = (1, 64, 256)
        I = 192
        E = 32
        K = 4
        SCALE = 1.8
        b, s, h = x.shape
        xf = x.reshape(-1, h).astype(jnp.float32)
        logits = xf @ router_w.T + router_b
        top_vals, top_idx = jax.lax.top_k(logits, K)
        rw = jax.nn.softmax(top_vals, axis=-1) * SCALE
        combine = jnp.einsum('tke,tk->te', jax.nn.one_hot(top_idx, E, dtype=xf.dtype), rw)
        g = jax.nn.silu(jnp.einsum('th,eih->tei', xf, gate_w))
        u = jnp.einsum('th,eih->tei', xf, up_w)
        routed = jnp.einsum('tei,ehi,te->th', g * u, down_w, combine)
        sg = jax.nn.silu(xf @ shared_gate_w.T)
        su = xf @ shared_up_w.T
        shared = sg * su @ shared_down_w.T
        return (routed + shared).reshape(b, s, h)
    x = x + _L0_xattn_ref(_layernorm(x, axis=-1), ctx_512, L0_xattn_W_k, L0_xattn_b_k, L0_xattn_ln_gamma, L0_xattn_ln_beta)
    x = x + _L0_ffn_ref(_layernorm(x, axis=-1), L0_ffn_router_w, L0_ffn_router_b, L0_ffn_gate_w, L0_ffn_up_w, L0_ffn_down_w, L0_ffn_shared_gate_w, L0_ffn_shared_up_w, L0_ffn_shared_down_w)
    return x

_drawn_inputs = setup_inputs


def setup_inputs(seed=0):
    import zlib

    import numpy as np

    out = dict(_drawn_inputs(seed))
    spreads = {'L0_xattn_b_k': (0.0, 0.8),
     'L0_xattn_ln_gamma': (1.0, 0.6),
     'L0_xattn_ln_beta': (0.0, 0.8),
     'L0_ffn_router_b': (0.0, 0.1)}
    factors = {'L0_xattn_W_k': 4.379}
    for name, (base, spread) in spreads.items():
        noise = np.random.default_rng([zlib.crc32(name.encode()), seed]).standard_normal(out[name].shape)
        drawn = base * np.exp(spread * noise) if base else spread * noise
        out[name] = jnp.asarray(drawn.astype(out[name].dtype))
    for name, factor in factors.items():
        out[name] = (out[name] * factor).astype(out[name].dtype)
    return out
```

```python
from contextlib import ExitStack

import concourse.bass as bass
from concourse import mybir

F32 = mybir.dt.float32
BF16 = mybir.dt.bfloat16
I32 = mybir.dt.int32
U32 = mybir.dt.uint32
ALU = mybir.AluOpType
ACT = mybir.ActivationFunctionType
AX = mybir.AxisListType

P = 128
B, S, H = 4, 256, 256
D = 64
NE, TOPK, I = 32, 4, 192
ROUTED_SCALE = 1.8
T = B * S
NT = T // P
TB = S // P
HALF = NT // 2
RSQRT_BITS = 0x5F3759DF
HC = H // P
IH = I // 2
GU = 2 * I
ROW = H + NE
SPILL = 32
TILES = NE + SPILL
AHEAD = 6
RING = 4
QUADS = NE // RING
SHARED = NE
LATE = 20
LN_EPS, SIM_EPS = 1e-5, 1e-6
SIM_SCALE = float(H) ** -0.5


def build(nc, x, ctxT, wkT, bk, gamma, beta, routerT, router_b, w_gu, w_dn, out):
    es = ExitStack()
    with es:
        def sb(name, shape, dt=F32):
            return es.enter_context(nc.sbuf_tensor(name, shape, dt))

        def pb(name):
            return es.enter_context(nc.psum_tensor(name, [P, 512], F32))

        def sem(name):
            return es.enter_context(nc.semaphore(name))

        rows_d = nc.dram_tensor("rows_d", [T + P, ROW], F32, kind="Internal").ap()
        acc_d = [nc.dram_tensor(f"acc{n}_d", [T + P, H], F32, kind="Internal").ap() for n in range(2)]

        wgu = sb("wgu", [P, (NE + 1) * HC * GU])
        wdn = sb("wdn", [P, (NE + 1) * 2 * H])

        SCRATCH = (NE - LATE) * HC * GU
        at = [0]

        def scratch(parts, words, dt=F32):
            a = wgu[0:parts, LATE * HC * GU + at[0]:LATE * HC * GU + at[0] + words]
            at[0] += words
            assert at[0] <= SCRATCH
            return a if dt == F32 else a.bitcast(dt)

        ctxT_s = scratch(D + 1, T)
        wkT_s = scratch(D + 1, D)
        kvT = scratch(D, T)
        kv = scratch(P, NT * D)
        outT = scratch(D, T)
        gam = scratch(P, S)
        bet = scratch(P, S)
        z1 = scratch(P, 2 * S).rearrange("p (b s) -> p b s", b=2)
        z2 = scratch(P, NT * S).rearrange("p (k s) -> p k s", k=NT)
        logits = scratch(P, NT * NE).rearrange("p (k e) -> p k e", k=NT)
        stats = scratch(P, NT * 6).rearrange("p (k s) -> p k s", k=NT)
        mv_s = scratch(P, NT * 2).rearrange("p (k s) -> p k s", k=NT)
        rs_s = scratch(P, NT)
        newton = scratch(P, 3 * HALF).rearrange("p (v k) -> p v k", v=3)
        at[0] = 0
        NC = NT * TOPK
        oh = scratch(P, NC * NE // 2, BF16)
        prod = scratch(P, NC * NE)
        eqj = scratch(P, NC * TILES // 2, BF16)
        lists = scratch(P, NC * 2 * TILES // 2, BF16)
        eqr = scratch(P, NC * P // 2, BF16)
        cum = scratch(P, (NT + 1) * NE).rearrange("p (k e) -> p k e", k=NT + 1)
        slot = scratch(P, NT * NE).rearrange("p (k e) -> p k e", k=NT)
        slot_a = scratch(P, NT * NE).rearrange("p (k e) -> p k e", k=NT)
        slot_b = scratch(P, NT * NE).rearrange("p (k e) -> p k e", k=NT)
        over_i = scratch(P, NE, I32)
        over_f = scratch(P, NE)
        pre = scratch(P, 2 * (16 + NE)).rearrange("p (b e) -> p b e", b=2)
        jump = scratch(P, NE)
        place = scratch(P, NC)
        place_i = scratch(P, 3 * NC, I32).rearrange("p (v n) -> p v n", v=3)
        place_f = scratch(P, 2 * NC).rearrange("p (v n) -> p v n", v=2)
        idx_pk = scratch(P, 2 * TILES).rearrange("p (v j) -> p v j", v=2)
        idx_a = scratch(P, TILES)
        idx_b = scratch(P, TILES)
        tile_e = scratch(P, TILES + 2)
        oh4 = oh.rearrange("p (k c e) -> p k c e", k=NT, c=TOPK)
        prod4 = prod.rearrange("p (k c e) -> p k c e", k=NT, c=TOPK)
        prod3 = prod.rearrange("p (n e) -> p n e", n=NC)
        eqj3 = eqj.rearrange("p (n j) -> p n j", n=NC)
        lists4 = lists.rearrange("p (n v j) -> p n v j", n=NC, v=2)
        eqr3 = eqr.rearrange("p (n r) -> p n r", n=NC)

        xres = sb("xres", [P, NT, H])
        xn = sb("xn", [P, NT, ROW])
        xnT = sb("xnT", [P, HC, T])
        rt_w = sb("rt_w", [P, HC, NE])
        rt_b = sb("rt_b", [1, NE])
        ones_row = sb("ones_row", [1, P])
        ident = sb("ident", [P, P])
        lower = sb("lower", [P, P], BF16)
        ones = sb("ones", [P, P], BF16)
        iota_f = sb("iota_f", [P, P])
        iota_b = sb("iota_b", [P, P], BF16)
        pcol = sb("pcol", [P, 1])
        dummy = sb("dummy_row", [P, 1])
        tile_no = sb("tile_no", [P, NT, TOPK], BF16)
        mv = sb("mv", [P, NT, 2])
        rs = sb("rs", [P, NT])
        nmax = sb("nmax", [P, NT])
        esum = sb("esum", [P, NT])
        rsum = sb("rsum", [P, NT])
        top = sb("top", [P, NT, 8])
        topi = sb("topi", [P, NT, 8], U32)
        w4 = sb("w4", [P, NT, TOPK])
        wsum = sb("wsum", [P, NT])
        idxf = sb("idxf", [P, NT, TOPK])
        idx = sb("idx", [P, TILES + AHEAD], I32)
        tile_ei = sb("tile_ei", [P, TILES + 2], I32)
        tile_oh = sb("tile_oh", [P, (TILES + 2) * NE], BF16)
        pairs = sb("pairs", [P, 2], I32)
        xn_flat = xn[:, :, :].rearrange("p k r -> p (k r)")
        xg = [xn_flat[:, u * ROW:(u + 1) * ROW] for u in range(RING)]
        xgT = [xn_flat[:, RING * ROW + b * HC * P:RING * ROW + (b + 1) * HC * P].rearrange("p (c t) -> p c t", c=HC)
               for b in range(2)]
        junk_at = RING * ROW + 2 * HC * P
        junk = [xn_flat[:, junk_at + u * NE:junk_at + (u + 1) * NE] for u in range(RING)]
        sg = sb("sg", [P, 2, I])
        h = sb("h", [P, 2, I])
        hT = sb("hT", [IH, 2, 2, P])
        y = sb("y", [P, RING, H])
        wcol = sb("wcol", [P, RING])
        gather_list = sb("gather_list", [P, RING], I32)
        add_list = sb("add_list", [P, RING], I32)

        ps_x = [pb(f"ps_x{n}") for n in range(2)]
        ps_g = [pb(f"ps_g{n}") for n in range(2)]
        ps_h = [pb(f"ps_h{n}") for n in range(2)]
        ps_y = [pb(f"ps_y{n}") for n in range(2)]

        x_in = [sem(f"x_in{n}") for n in range(2)]
        ctx_in, affine_in, router_in = sem("ctx_in"), sem("affine_in"), sem("router_in")
        w_shared, w_early, w_late = sem("w_shared"), sem("w_early"), sem("w_late")
        dve_const, pool_const, zeroed = sem("dve_const"), sem("pool_const"), sem("zeroed")
        xn_ready = sem("xn_ready")
        xT_done, xT_copied = sem("xT_done"), sem("xT_copied")
        kvT_done, kv_done, kv_copied = sem("kvT_done"), sem("kv_done"), sem("kv_copied")
        oT_done, oT_copied = sem("oT_done"), sem("oT_copied")
        sim_done, sim_read, z_ready, exp_done = sem("sim_done"), sem("sim_read"), sem("z_ready"), sem("exp_done")
        x2_ready, logit_done, logit_copied = sem("x2_ready"), sem("logit_done"), sem("logit_copied")
        top_ready, wexp_done, w_ready, rows_in = sem("top_ready"), sem("wexp_done"), sem("w_ready"), sem("rows_in")
        oh_ready, rank_done = sem("oh_ready"), sem("rank_done")
        eqj_ready, tile_part, places_ready, idx_done = sem("eqj_ready"), sem("tile_part"), sem("places_ready"), sem("idx_done")
        idx_ready, spill_ready = sem("idx_ready"), sem("spill_ready")
        dve_step, pool_step, turns = sem("dve_step"), sem("pool_step"), sem("turns")
        s_gu, s_silu, s_mul, s_hT, s_hTc, s_dn, s_sum = (
            sem(n) for n in ("s_gu", "s_silu", "s_mul", "s_hT", "s_hTc", "s_dn", "s_sum"))
        r_xT, r_xTc, r_w, r_gu, r_silu, r_mul, r_hT, r_hTc, r_dn, r_y = (
            sem(n) for n in ("r_xT", "r_xTc", "r_w", "r_gu", "r_silu", "r_mul", "r_hT", "r_hTc", "r_dn", "r_y"))
        gathered = [sem(f"gathered{n}") for n in range(RING)]
        added = [sem(f"added{n}") for n in range(2)]
        acc_in, final, out_done = [sem(f"acc_in{n}") for n in range(4)], sem("final"), sem("out_done")

        def w_up(e, c):
            if isinstance(e, int):
                return wgu[:, (e * HC + c) * GU:(e * HC + c + 1) * GU]
            return wgu[:, bass.ds(e * (HC * GU) + c * GU, GU)]

        def w_down(e, c):
            if isinstance(e, int):
                return wdn[0:IH, (e * 2 + c) * H:(e * 2 + c + 1) * H]
            return wdn[0:IH, bass.ds(e * (2 * H) + c * H, H)]

        block = es.enter_context(nc.Block())

        @block.sync
        def _(sp):
            xv = x.rearrange("(k p) h -> p k h", p=P)
            sp.dma_start(xres[:, 0:4, :], xv[:, 0:4, :]).then_inc(x_in[0], 16)
            sp.dma_start(ctxT_s[0:D, :], ctxT).then_inc(ctx_in, 16)
            sp.dma_start(wkT_s[0:D, :], wkT).then_inc(ctx_in, 16)
            sp.dma_start(wkT_s[D:D + 1, :], bk).then_inc(ctx_in, 16)
            sp.dma_start(xres[:, 4:8, :], xv[:, 4:8, :]).then_inc(x_in[1], 16)
            sp.dma_start(gam, gamma.to_broadcast([P, S])).then_inc(affine_in, 16)
            sp.dma_start(bet, beta.to_broadcast([P, S])).then_inc(affine_in, 16)
            sp.dma_start(rt_w[:, :, :], routerT).then_inc(router_in, 16)
            sp.dma_start(rt_b[:, :], router_b).then_inc(router_in, 16)

            def load_weights(a, b, done):
                sp.dma_start(wgu[:, a * HC * GU:b * HC * GU], w_gu[:, a * HC * GU:b * HC * GU]).then_inc(done, 16)
                sp.dma_start(wdn[0:IH, a * 2 * H:b * 2 * H], w_dn[:, a * 2 * H:b * 2 * H]).then_inc(done, 16)

            load_weights(SHARED, SHARED + 1, w_shared)
            for e in range(0, LATE, RING):
                load_weights(e, e + RING, w_early)
                if e == 0:
                    sp.wait_ge(dve_const, 1)
                    zeros = y[:, :, :].rearrange("p u h -> p (u h)")
                    for acc in acc_d:
                        av = acc.rearrange("(p a) h -> p (a h)", p=P)
                        for n in range(3):
                            words = min(RING * H, 9 * H - n * RING * H)
                            sp.dma_start(av[:, n * RING * H:n * RING * H + words], zeros[:, 0:words]).then_inc(zeroed, 16)
                    sp.dma_start(rows_d[T:T + P, :], zeros[:, 0:ROW]).then_inc(zeroed, 16)
            rv = rows_d[0:T, :].rearrange("(k p) h -> p k h", p=P)
            for n in range(2):
                sp.wait_ge(x2_ready, 4 * n + 4)
                sp.dma_start(rv[:, 4 * n:4 * n + 4, 0:H], xn[:, 4 * n:4 * n + 4, 0:H]).then_inc(rows_in, 16)
            sp.wait_ge(w_ready, 1)
            sp.dma_start(rv[:, :, H:ROW], xn[:, :, H:ROW]).then_inc(rows_in, 16)
            sp.wait_ge(idx_done, 1)
            sp.wait_ge(spill_ready, 1)
            load_weights(LATE, NE, w_late)
            n_pairs = nc.sync.value_load(pairs[0:1, 1:2], min_val=0, max_val=SPILL // 2)
            for b in range(2):
                sp.wait_ge(added[b], n_pairs * 16 + 16 * NE // 2)
            for u in range(RING):
                sp.wait_ge(gathered[u], ((n_pairs * 2 + (NE + AHEAD + RING - 1 - u)) >> 2) * 16)
            av = [a[0:T, :].rearrange("(k p) h -> p k h", p=P) for a in acc_d]
            into = [xnT[:, :, :].rearrange("p c (k h) -> p (c k) h", h=H), xn[:, :, 0:H]]
            for q in range(4):
                for n in range(2):
                    sp.dma_start(into[n][:, 2 * q:2 * q + 2, :], av[n][:, 2 * q:2 * q + 2, :]).then_inc(acc_in[q], 16)
            ov = out.rearrange("(k p) h -> p k h", p=P)
            for q in range(4):
                sp.wait_ge(final, q + 1)
                sp.dma_start(ov[:, 2 * q:2 * q + 2, :], xres[:, 2 * q:2 * q + 2, :]).then_inc(out_done, 16)
            sp.wait_ge(out_done, 64)

        @block.gpsimd
        def _(pool):
            g = nc.gpsimd
            g.memset(ident[:, :], 0.0).then_inc(pool_step, 1)
            g.memset(lower[:, :], 1.0).then_inc(pool_step, 1)
            g.memset(ones[:, :], 1.0)
            pool.wait_ge(pool_step, 2)
            g.affine_select(out=ident[:, :], in_=ident[:, :], compare_op=ALU.not_equal, fill=1.0,
                            base=0, pattern=[[-1, P]], channel_multiplier=1)
            g.affine_select(out=lower[:, :], in_=lower[:, :], compare_op=ALU.is_gt, fill=0.0,
                            base=0, pattern=[[1, P]], channel_multiplier=-1)
            g.iota(iota_f[:, :], pattern=[[1, P]], base=0, channel_multiplier=0, allow_small_or_imprecise_dtypes=True)
            g.iota(iota_b[:, :], pattern=[[1, P]], base=0, channel_multiplier=0, allow_small_or_imprecise_dtypes=True)
            g.iota(pcol[:, :], pattern=[[0, 1]], base=0, channel_multiplier=1, allow_small_or_imprecise_dtypes=True)
            g.iota(dummy[:, :], pattern=[[0, 1]], base=T + P, channel_multiplier=1, allow_small_or_imprecise_dtypes=True)
            g.iota(idx[:, TILES:TILES + AHEAD], pattern=[[0, AHEAD]], base=T, channel_multiplier=1)
            g.iota(tile_no[:, :, :], pattern=[[1, NT], [0, TOPK]], base=1, channel_multiplier=0,
                   allow_small_or_imprecise_dtypes=True).then_inc(pool_const, 1)
            pool.wait_ge(eqj_ready, 1)
            g.tensor_tensor(lists4[:, :, 1, :], eqj3, tile_no[:, :, :].rearrange("p k c -> p (k c)").unsqueeze(2)
                            .to_broadcast([P, NC, TILES]), ALU.mult).then_inc(tile_part, 1)

            def gather(u, column):
                g.indirect_dma_start(xg[u], None, rows_d, bass.IndirectOffsetOnAxis(ap=column, axis=0)).then_inc(gathered[u], 16)

            def step(j, u):
                pool.wait_ge(r_y, j + 1)
                if not isinstance(j, int) or j >= 2:
                    pool.wait_ge(added[u % 2], (j // 2) * 16 if isinstance(j, int) else (j - u) * 8 + 16 * (u // 2))
                pool.sem_inc(turns, 1)
                g.indirect_dma_start(acc_d[u % 2], bass.IndirectOffsetOnAxis(ap=add_list[:, u:u + 1], axis=0), y[:, u, :], None,
                                     compute_op=ALU.add).then_inc(added[u % 2], 16)
                pool.wait_ge(r_xT, j + 3)
                pool.wait_ge(r_w, j + 3)
                pool.sem_inc(turns, 1)
                n = (u + AHEAD) % RING
                gather(n, gather_list[:, n:n + 1])

            pool.wait_ge(zeroed, 16 * 7)
            pool.wait_ge(rows_in, 16 * 3)
            pool.wait_ge(idx_ready, 1)
            for j in range(RING):
                gather(j, idx[:, j:j + 1])
            for j in range(RING, AHEAD):
                pool.wait_ge(r_xT, j - RING + 1)
                pool.wait_ge(r_w, j - RING + 1)
                gather(j % RING, idx[:, j:j + 1])
            for u in range(RING):
                step(u, u)
            with pool.Fori(1, QUADS) as i:
                for u in range(RING):
                    step(i * RING + u, u)
            pool.wait_ge(spill_ready, 1)
            n_pairs = g.value_load(pairs[0:1, 1:2], min_val=0, max_val=SPILL // 2)
            with pool.Fori(QUADS, 2 * QUADS) as i:
                for pair in range(2):
                    with pool.If(i * 2 + (pair - 2 * QUADS) < n_pairs):
                        for u in (2 * pair, 2 * pair + 1):
                            step(i * RING + u, u)

        @block.scalar
        def _(act):
            a = nc.scalar
            for n in range(2):
                act.wait_ge(kvT_done, n + 1)
                a.activation(kvT[:, n * 512:(n + 1) * 512], ps_h[n][0:D, :], ACT.Copy).then_inc(kv_copied, 1)
            act.wait_ge(kv_done, 1)
            a.activation(kv, ps_y[0][:, :], ACT.Copy).then_inc(kv_copied, 1)

            def copy_xT(n):
                k = n % NT
                act.wait_ge(xT_done, n + 1)
                a.activation(xnT[:, :, k * P:(k + 1) * P], ps_x[n % 2][:, 0:HC * P].rearrange("p (c t) -> p c t", c=HC),
                             ACT.Copy).then_inc(xT_copied, 1)

            def copy_outT(b):
                act.wait_ge(oT_done, b + 1)
                a.activation(outT[:, b * S:(b + 1) * S], ps_y[(b + 1) % 2][0:D, 0:S], ACT.Copy,
                             scale=SIM_SCALE).then_inc(oT_copied, 1)

            for n in range(2):
                for k in range(n * HALF, (n + 1) * HALF):
                    copy_xT(k)
                for b in range(2 * n, 2 * n + 2):
                    copy_outT(b)
            for k in range(NT):
                act.wait_ge(z_ready, k + 1)
                a.activation(z2[:, k, :], z2[:, k, :], ACT.Exp, bias=nmax[:, k:k + 1],
                             accum_out=esum[:, k:k + 1]).then_inc(exp_done, 1)
            for k in range(NT + 1):
                if k < NT:
                    copy_xT(NT + k)
                if k >= 1:
                    act.wait_ge(logit_done, k)
                    a.activation(logits[:, k - 1, :], ps_h[(k - 1) % 2][:, 0:NE], ACT.Copy).then_inc(logit_copied, 1)
            act.wait_ge(top_ready, 1)
            a.activation(w4[:, :, :], w4[:, :, :], ACT.Exp).then_inc(wexp_done, 1)

            for s in range(NT):
                act.wait_ge(s_gu, s + 1)
                if s >= 2:
                    act.wait_ge(s_mul, s - 1)
                a.activation(sg[:, s % 2, :], ps_g[s % 2][:, 0:I], ACT.Silu).then_inc(s_silu, 1)
                act.wait_ge(s_hT, s + 1)
                a.activation(hT[:, s % 2, :, :], ps_h[s % 2][0:IH, 0:2 * P].rearrange("p (c t) -> p c t", c=2),
                             ACT.Copy).then_inc(s_hTc, 1)

            def copy_rows_T(j, b):
                act.wait_ge(r_xT, j + 1)
                a.activation(xgT[b], ps_x[b][:, 0:HC * P].rearrange("p (c t) -> p c t", c=HC), ACT.Copy).then_inc(r_xTc, 1)

            def step(j, u):
                b = u % 2
                act.wait_ge(r_gu, j + 1)
                if not isinstance(j, int) or j >= 2:
                    act.wait_ge(r_mul, j - 1)
                a.activation(sg[:, b, :], ps_g[b][:, 0:I], ACT.Silu).then_inc(r_silu, 1)
                copy_rows_T(j + 2, b)
                act.wait_ge(r_hT, j + 1)
                a.activation(hT[:, b, :, :], ps_h[b][0:IH, 0:2 * P].rearrange("p (c t) -> p c t", c=2),
                             ACT.Copy).then_inc(r_hTc, 1)

            copy_rows_T(0, 0)
            copy_rows_T(1, 1)
            for u in range(RING):
                step(u, u)
            with act.Fori(1, QUADS) as i:
                for u in range(RING):
                    step(i * RING + u, u)
            act.wait_ge(spill_ready, 1)
            n_pairs = a.value_load(pairs[0:1, 1:2], min_val=0, max_val=SPILL // 2)
            with act.Fori(QUADS, 2 * QUADS) as i:
                for pair in range(2):
                    with act.If(i * 2 + (pair - 2 * QUADS) < n_pairs):
                        for u in (2 * pair, 2 * pair + 1):
                            step(i * RING + u, u)

        @block.tensor
        def _(pe):
            t = nc.tensor
            pe.wait_ge(ctx_in, 48)
            pe.wait_ge(dve_const, 2)
            for n in range(2):
                t.matmul(ps_h[n][0:D, :], wkT_s, ctxT_s[:, n * 512:(n + 1) * 512], start=True, stop=True).then_inc(kvT_done, 1)
            for k in range(NT):
                last = t.matmul(ps_y[0][:, k * D:(k + 1) * D], ctxT_s[:, k * P:(k + 1) * P], wkT_s, start=True, stop=True)
            last.then_inc(kv_done, 1)

            def transpose_x(n):
                k = n % NT
                if n < NT:
                    pe.wait_ge(xn_ready, n + 1)
                else:
                    pe.wait_ge(x2_ready, k + 1)
                if n >= 2:
                    pe.wait_ge(xT_copied, n - 1)
                for c in range(HC):
                    last = t.transpose(ps_x[n % 2][:, c * P:(c + 1) * P], xn[:, k, c * P:(c + 1) * P], ident[:, :])
                last.then_inc(xT_done, 1)

            def attend(b):
                pe.wait_ge(xT_copied, 2 * b + 2)
                pe.wait_ge(kv_copied, 3)
                if b >= 2:
                    pe.wait_ge(oT_copied, b - 1)
                for c in range(TB):
                    k = TB * b + c
                    last = t.matmul(ps_y[(b + 1) % 2][0:D, 0:S], kv[:, k * D:(k + 1) * D], xnT[:, c, b * S:(b + 1) * S],
                                    start=(c == 0), stop=(c == TB - 1))
                last.then_inc(oT_done, 1)

            def sim_bank(k):
                return (ps_g, ps_y)[k // HALF][k % HALF // 2][:, k % 2 * S:(k % 2 + 1) * S]

            def similarity(k):
                b = k // TB
                pe.wait_ge(oT_copied, b + 1 if k < HALF else B)
                t.matmul(sim_bank(k), outT[:, k * P:(k + 1) * P], kvT[:, b * S:(b + 1) * S],
                         start=True, stop=True).then_inc(sim_done, 1)

            def route(k):
                pe.wait_ge(xT_copied, NT + k + 1)
                if k == 0:
                    pe.wait_ge(router_in, 32)
                if k >= 2:
                    pe.wait_ge(logit_copied, k - 1)
                for c in range(HC):
                    t.matmul(ps_h[k % 2][:, 0:NE], xnT[:, c, k * P:(k + 1) * P], rt_w[:, c, :], start=(c == 0), stop=False)
                t.matmul(ps_h[k % 2][:, 0:NE], ones_row[:, :], rt_b[:, :], start=False, stop=True).then_inc(logit_done, 1)

            pe.wait_ge(pool_const, 1)
            for k in range(HALF):
                transpose_x(k)
            for b in range(2):
                attend(b)
                similarity(2 * b)
                similarity(2 * b + 1)
            for k in range(HALF, NT):
                transpose_x(k)
            attend(2)
            attend(3)
            for k in range(HALF, NT):
                similarity(k)
            for k in range(NT + 1):
                if k < NT:
                    transpose_x(NT + k)
                if k >= 1:
                    route(k - 1)

            def shared_up(s):
                if s == 0:
                    pe.wait_ge(sim_read, NT)
                if s >= 2:
                    pe.wait_ge(s_mul, s - 1)
                for c in range(HC):
                    last = t.matmul(ps_g[s % 2][:, 0:GU], xnT[:, c, s * P:(s + 1) * P], w_up(SHARED, c),
                                    start=(c == 0), stop=(c == HC - 1))
                last.then_inc(s_gu, 1)

            def shared_transpose(s):
                pe.wait_ge(s_mul, s + 1)
                pe.wait_ge(logit_copied, NT)
                for c in range(2):
                    last = t.transpose(ps_h[s % 2][0:IH, c * P:(c + 1) * P], h[:, s % 2, c * IH:(c + 1) * IH], ident[:, :])
                last.then_inc(s_hT, 1)

            def shared_down(s):
                pe.wait_ge(s_hTc, s + 1)
                if s >= 2:
                    pe.wait_ge(s_sum, s - 1)
                for c in range(2):
                    last = t.matmul(ps_y[s % 2][:, 0:H], hT[:, s % 2, c, :], w_down(SHARED, c), start=(c == 0), stop=(c == 1))
                last.then_inc(s_dn, 1)

            def rank():
                pe.wait_ge(oh_ready, 1)
                pe.wait_ge(xT_copied, 2 * NT)
                for part, m in enumerate((lower, ones)):
                    for c in range(TOPK):
                        last = t.matmul(ps_x[0][:, part * NT * NE:(part + 1) * NT * NE], m[:, :], oh4[:, :, c, :],
                                        start=(c == 0), stop=(c == TOPK - 1))
                last.then_inc(rank_done, 1)

            def make_lists():
                pe.wait_ge(places_ready, 1)
                pe.wait_ge(tile_part, 1)
                for n in range(NC):
                    last = t.matmul(ps_x[1][:, 0:2 * TILES], eqr3[:, n, :], lists4[:, n, :, :], start=(n == 0), stop=(n == NC - 1))
                last.then_inc(idx_done, 1)

            pe.wait_ge(w_shared, 32)
            for s in range(NT):
                shared_up(s)
                if s >= 1:
                    shared_down(s - 1)
                shared_transpose(s)
                if s == 1:
                    rank()
                if s == 6:
                    make_lists()
            shared_down(NT - 1)

            def rows_T(j, b, u, count):
                pe.wait_ge(gathered[u], count)
                if not isinstance(j, int) or j >= 2:
                    pe.wait_ge(r_xTc, j - 1)
                for c in range(HC):
                    last = t.transpose(ps_x[b][:, c * P:(c + 1) * P], xg[u][:, c * P:(c + 1) * P], ident[:, :])
                last.then_inc(r_xT, 1)

            def down(j, b, e):
                pe.wait_ge(r_hTc, j + 1)
                if not isinstance(j, int) or j >= 2:
                    pe.wait_ge(r_y, j - 1)
                for c in range(2):
                    last = t.matmul(ps_y[b][:, 0:H], hT[:, b, c, :], w_down(e, c), start=(c == 0), stop=(c == 1))
                last.then_inc(r_dn, 1)

            def step(j, u, e, e_before):
                b = u % 2
                pe.wait_ge(r_xTc, j + 1)
                if not isinstance(j, int) or j >= 2:
                    pe.wait_ge(r_mul, j - 1)
                for c in range(HC):
                    last = t.matmul(ps_g[b][:, 0:GU], xgT[b][:, c, :], w_up(e, c), start=(c == 0), stop=(c == HC - 1))
                last.then_inc(r_gu, 1)
                if not isinstance(j, int) or j >= 1:
                    down(j - 1, 1 - b, e_before)
                nxt = (u + 2) % RING
                rows_T(j + 2, b, nxt, (j - u) * 4 + 16 * ((u + 2) // RING + 1))
                pe.wait_ge(r_mul, j + 1)
                for c in range(2):
                    last = t.transpose(ps_h[b][0:IH, c * P:(c + 1) * P], h[:, b, c * IH:(c + 1) * IH], ident[:, :])
                last.then_inc(r_hT, 1)

            pe.wait_ge(w_early, 32 * LATE // RING)
            pe.wait_ge(idx_ready, 1)
            pe.wait_ge(s_sum, NT)
            rows_T(0, 0, 0, 16)
            rows_T(1, 1, 1, 16)
            for u in range(RING):
                step(u, u, u, u - 1)
            with pe.Fori(1, LATE // RING) as i:
                for u in range(RING):
                    step(i * RING + u, u, i * RING + u, i * RING + (u - 1))
            pe.wait_ge(w_late, 32)
            with pe.Fori(LATE // RING, QUADS) as i:
                for u in range(RING):
                    step(i * RING + u, u, i * RING + u, i * RING + (u - 1))
            pe.wait_ge(spill_ready, 1)
            n_pairs = t.value_load(pairs[0:1, 1:2], min_val=0, max_val=SPILL // 2)
            with pe.Fori(QUADS, 2 * QUADS) as i:
                for pair in range(2):
                    with pe.If(i * 2 + (pair - 2 * QUADS) < n_pairs):
                        j = i * RING + 2 * pair
                        e = [t.value_load(tile_ei[0:1, bass.ds(j + n, 1)], min_val=0, max_val=NE - 1) for n in (-1, 0, 1)]
                        step(j, 2 * pair, e[1], e[0])
                        step(j + 1, 2 * pair + 1, e[2], e[1])
            n_tiles = n_pairs * 2 + NE
            e_last = t.value_load(tile_ei[0:1, bass.ds(n_tiles - 1, 1)], min_val=0, max_val=NE - 1)
            down(n_tiles - 1, 1, e_last)

        @block.vector
        def _(dve):
            v = nc.vector
            steps = [0]

            def step_of(ins):
                steps[0] += 1
                ins.then_inc(dve_step, 1)
                return steps[0]

            def link(ins):
                dve.wait_ge(dve_step, step_of(ins))

            v.memset(y[:, :, :], 0.0).then_inc(dve_const, 1)
            v.memset(ctxT_s[D:D + 1, :], 1.0).then_inc(dve_const, 1)
            v.memset(ones_row[:, :], 1.0)
            v.memset(pre[:, :, :], 0.0)

            def rsqrt(where, variance, eps):
                arg, y0, part = newton[:, 0, :], where, newton[:, 1, :]
                link(v.tensor_scalar(arg, variance, eps, None, ALU.add))
                link(v.tensor_scalar(newton[:, 2, :].bitcast(I32), arg.bitcast(I32), 1, None, ALU.arith_shift_right))
                link(v.tensor_scalar(y0.bitcast(I32), newton[:, 2, :].bitcast(I32), -1.0, float(RSQRT_BITS), ALU.mult, ALU.add))
                for n in range(3):
                    link(v.scalar_tensor_tensor(part, y0, -0.5, y0, ALU.mult, ALU.mult))
                    link(v.tensor_tensor(part, part, arg, ALU.mult))
                    last = v.scalar_tensor_tensor(y0, part, 1.5, y0, ALU.add, ALU.mult)
                    if n < 2:
                        link(last)
                return last

            def variances(m, n):
                return m[:, n * HALF:(n + 1) * HALF, 1:2].rearrange("p k o -> p (k o)")

            def normalise(k, done):
                v.tensor_scalar(xn[:, k, 0:H], xres[:, k, :], mv[:, k, 0:1], rs[:, k:k + 1],
                                ALU.subtract, ALU.mult).then_inc(done, 1)

            for n in range(2):
                half = range(n * HALF, (n + 1) * HALF)
                dve.wait_ge(x_in[n], 16)
                for k in half:
                    last = v.bn_stats(stats[:, k, :], xres[:, k, :])
                link(last)
                for k in half:
                    last = v.bn_aggr(mv[:, k, :], stats[:, k, :])
                link(last)
                link(rsqrt(rs[:, n * HALF:(n + 1) * HALF], variances(mv, n), LN_EPS))
                for k in half:
                    normalise(k, xn_ready)

            dve.wait_ge(affine_in, 32)
            for n in range(2):
                half = range(n * HALF, (n + 1) * HALF)
                sim = {k: (ps_g, ps_y)[n][k % HALF // 2][:, k % 2 * S:(k % 2 + 1) * S] for k in half}
                for k in half:
                    dve.wait_ge(sim_done, k // 2 * 2 + 2)
                    last = v.bn_stats(stats[:, k, :], sim[k])
                link(last)
                for k in half:
                    last = v.bn_aggr(mv_s[:, k, :], stats[:, k, :])
                link(last)
                link(rsqrt(rs_s[:, n * HALF:(n + 1) * HALF], variances(mv_s, n), SIM_EPS))
                z2_step = {}
                for k in [*half, None]:
                    if k is not None:
                        if k - 2 in half:
                            dve.wait_ge(dve_step, z2_step[k - 2])
                        v.scalar_tensor_tensor(z1[:, k % 2, :], sim[k], mv_s[:, k, 0:1], gam, ALU.subtract, ALU.mult).then_inc(sim_read, 1)
                    before = (n + 1) * HALF - 1 if k is None else k - 1
                    if before in half:
                        dve.wait_ge(sim_read, before + 1)
                        z2_step[before] = step_of(v.scalar_tensor_tensor(
                            z2[:, before, :], z1[:, before % 2, :], rs_s[:, before:before + 1], bet, ALU.mult, ALU.add))
                    if before - 1 in half:
                        dve.wait_ge(dve_step, z2_step[before - 1])
                        v.tensor_reduce(nmax[:, before - 1:before], z2[:, before - 1, :], AX.X, ALU.max, negate=True).then_inc(z_ready, 1)
                dve.wait_ge(dve_step, z2_step[half[-1]])
                v.tensor_reduce(nmax[:, half[-1]:half[-1] + 1], z2[:, half[-1], :], AX.X, ALU.max, negate=True).then_inc(z_ready, 1)

            for n in range(2):
                half = range(n * HALF, (n + 1) * HALF)
                dve.wait_ge(exp_done, (n + 1) * HALF)
                link(v.reciprocal(rsum[:, half[0]:half[0] + HALF], esum[:, half[0]:half[0] + HALF]))
                dve.wait_ge(xn_ready, (n + 1) * HALF)
                for k in half:
                    last = v.scalar_tensor_tensor(xres[:, k, :], z2[:, k, :], rsum[:, k:k + 1], xres[:, k, :], ALU.mult, ALU.add)
                link(last)
                for k in half:
                    last = v.bn_stats(stats[:, k, :], xres[:, k, :])
                link(last)
                for k in half:
                    last = v.bn_aggr(mv[:, k, :], stats[:, k, :])
                link(last)
                link(rsqrt(rs[:, n * HALF:(n + 1) * HALF], variances(mv, n), LN_EPS))
                for k in half:
                    dve.wait_ge(xT_done, k + 1)
                    normalise(k, x2_ready)
            for k in range(NT):
                dve.wait_ge(logit_copied, k + 1)
                link(v.max(top[:, k, :], logits[:, k, :]))
                last = v.max_index(topi[:, k, :], top[:, k, :], logits[:, k, :])
            link(last)

            v.tensor_tensor(w4[:, :, :], top[:, :, 0:TOPK], top[:, :, 0:1].to_broadcast([P, NT, TOPK]),
                            ALU.subtract).then_inc(top_ready, 1)
            link(v.tensor_copy(idxf[:, :, :], topi[:, :, 0:TOPK]))
            dve.wait_ge(pool_const, 1)
            experts = iota_f[:, 0:NE].unsqueeze(1)
            v.tensor_tensor(oh.rearrange("p (n e) -> p n e", n=NC), experts.to_broadcast([P, NC, NE]),
                            idxf[:, :, :].rearrange("p k c -> p (k c)").unsqueeze(2).to_broadcast([P, NC, NE]),
                            ALU.is_equal).then_inc(oh_ready, 1)

            def shared_product(s):
                dve.wait_ge(s_silu, s + 1)
                v.tensor_tensor(h[:, s % 2, :], ps_g[s % 2][:, I:GU], sg[:, s % 2, :], ALU.mult).then_inc(s_mul, 1)

            def shared_sum(s):
                dve.wait_ge(s_dn, s + 1)
                v.tensor_tensor(xres[:, s, :], ps_y[s % 2][:, 0:H], xres[:, s, :], ALU.add).then_inc(s_sum, 1)

            shared_product(0)
            dve.wait_ge(wexp_done, 1)
            link(v.tensor_reduce(wsum[:, :], w4[:, :, :], AX.X, ALU.add))
            link(v.reciprocal(wsum[:, :], wsum[:, :]))
            link(v.scalar_tensor_tensor(w4[:, :, :], w4[:, :, :], ROUTED_SCALE,
                                        wsum[:, :].unsqueeze(2).to_broadcast([P, NT, TOPK]), ALU.mult, ALU.mult))
            shared_product(1)
            dve.wait_ge(oh_ready, 1)
            link(v.tensor_tensor(prod3, oh.rearrange("p (n e) -> p n e", n=NC),
                                 w4[:, :, :].rearrange("p k c -> p (k c)").unsqueeze(2).to_broadcast([P, NC, NE]), ALU.mult))
            v.tensor_reduce(xn[:, :, H:ROW], prod4.rearrange("p k c e -> p k e c"), AX.X, ALU.add).then_inc(w_ready, 1)
            shared_sum(0)
            shared_product(2)
            shared_sum(1)

            dve.wait_ge(rank_done, 1)
            ranks = ps_x[0][:, 0:NT * NE].rearrange("p (k e) -> p k e", k=NT)
            totals = ps_x[0][:, NT * NE:2 * NT * NE].rearrange("p (k e) -> p k e", k=NT)
            link(v.memset(cum[:, 0, :], 0.0))
            for k in range(NT):
                link(v.tensor_tensor(cum[:, k + 1, :], cum[:, k, :], totals[:, k, :], ALU.add))
            shared_product(3)
            link(v.tensor_scalar(over_i[:, :], cum[:, NT, :], float(P - 1), None, ALU.add))
            link(v.tensor_scalar(over_i[:, :], over_i[:, :], 7, None, ALU.arith_shift_right))
            link(v.tensor_scalar(over_f[:, :], over_i[:, :], -1.0, 0.0, ALU.add, ALU.max))
            link(v.tensor_copy(pre[:, 0, 16:], over_f[:, :]))
            for n in range(5):
                a, b = n % 2, 1 - n % 2
                link(v.tensor_tensor(pre[:, b, 16:], pre[:, a, 16:], pre[:, a, 16 - (1 << n):16 + NE - (1 << n)], ALU.add))
            incl = pre[:, 1, 16:]
            shared_sum(2)
            link(v.tensor_tensor(jump[:, :], incl, over_f[:, :], ALU.subtract))
            link(v.scalar_tensor_tensor(jump[:, :], jump[:, :], float(NE - 1), iota_f[:, 0:NE], ALU.add, ALU.subtract))
            link(v.tensor_scalar(jump[:, :], jump[:, :], float(P), None, ALU.mult))
            link(v.tensor_tensor(slot[:, :, :], ranks, cum[:, 0:NT, :], ALU.add))
            v.scalar_tensor_tensor(slot_a[:, :, :], slot[:, :, :], float(P), jump[:, :].unsqueeze(1).to_broadcast([P, NT, NE]),
                                   ALU.is_ge, ALU.mult)
            link(v.scalar_tensor_tensor(slot_b[:, :, :], experts.to_broadcast([P, NT, NE]), float(P), slot[:, :, :],
                                        ALU.mult, ALU.add))
            link(v.tensor_tensor(slot[:, :, :], slot_a[:, :, :], slot_b[:, :, :], ALU.add))
            shared_product(4)
            link(v.tensor_tensor(prod4, oh4, slot[:, :, :].unsqueeze(2).to_broadcast([P, NT, TOPK, NE]), ALU.mult))
            link(v.tensor_reduce(place[:, :], prod3, AX.X, ALU.add))
            link(v.tensor_copy(place_i[:, 0, :], place[:, :]))
            v.tensor_scalar(place_i[:, 1, :], place_i[:, 0, :], P - 1, None, ALU.bitwise_and)
            link(v.tensor_scalar(place_i[:, 2, :], place_i[:, 0, :], 7, None, ALU.arith_shift_right))
            link(v.tensor_copy(place_f[:, :, :], place_i[:, 1:3, :]))
            v.tensor_tensor(eqj3, iota_b[:, 0:TILES].unsqueeze(1).to_broadcast([P, NC, TILES]),
                            place_f[:, 1, :].unsqueeze(2).to_broadcast([P, NC, TILES]), ALU.is_equal).then_inc(eqj_ready, 1)
            shared_sum(3)
            shared_product(5)
            link(v.tensor_tensor(eqr3, iota_b[:, :].unsqueeze(1).to_broadcast([P, NC, P]),
                                 place_f[:, 0, :].unsqueeze(2).to_broadcast([P, NC, P]), ALU.is_equal))
            dve.wait_ge(eqj_ready, 1)
            v.tensor_scalar(lists4[:, :, 0, :], eqj3, pcol[:, :], None, ALU.mult).then_inc(places_ready, 1)
            shared_sum(4)
            shared_product(6)
            shared_sum(5)
            v.tensor_copy(tile_e[:, 0:NE], iota_f[:, 0:NE])
            link(v.tensor_tensor(prod3, incl.unsqueeze(1).to_broadcast([P, NC, NE]),
                                 iota_f[:, 0:SPILL].unsqueeze(2).to_broadcast([P, SPILL, NE]), ALU.is_le))
            v.memset(tile_e[:, TILES:], float(NE - 1))
            link(v.tensor_reduce(tile_e[:, NE:TILES], prod3, AX.X, ALU.add))
            link(v.tensor_scalar(tile_e[:, NE:TILES], tile_e[:, NE:TILES], float(NE - 1), None, ALU.min))
            shared_product(7)
            dve.wait_ge(idx_done, 1)
            link(v.tensor_copy(idx_pk[:, :, :], ps_x[1][:, 0:2 * TILES].rearrange("p (v j) -> p v j", v=2)))
            v.scalar_tensor_tensor(idx_a, idx_pk[:, 1, :], float(P), idx_pk[:, 0, :], ALU.mult, ALU.add)
            link(v.tensor_scalar(idx_b, idx_pk[:, 1, :], 0.0, dummy[:, :], ALU.is_equal, ALU.mult))
            v.scalar_tensor_tensor(idx[:, 0:TILES], idx_a, -float(P), idx_b, ALU.add, ALU.add).then_inc(idx_ready, 1)
            shared_sum(6)
            v.tensor_copy(tile_ei[:, :], tile_e[:, :])
            link(v.tensor_scalar(pairs[:, 0:1], pre[:, 1, 15 + NE:16 + NE], 1.0, None, ALU.add))
            link(v.tensor_tensor(tile_oh[:, :].rearrange("p (j e) -> p j e", e=NE), experts.to_broadcast([P, TILES + 2, NE]),
                                 tile_e[:, :].unsqueeze(2).to_broadcast([P, TILES + 2, NE]), ALU.is_equal))
            v.tensor_scalar(pairs[:, 1:2], pairs[:, 0:1], 1, None, ALU.arith_shift_right).then_inc(spill_ready, 1)
            shared_sum(7)

            def column(j):
                return idx[:, j:j + 1] if isinstance(j, int) else idx[:, bass.ds(j, 1)]

            def row_weight(j, u, count):
                dve.wait_ge(gathered[u], count)
                if not isinstance(j, int) or j >= AHEAD - RING:
                    v.tensor_copy(gather_list[:, u:u + 1], column(j + RING))
                if not isinstance(j, int) or j >= RING:
                    dve.wait_ge(r_y, j - RING + 1)
                one = tile_oh[:, j * NE:(j + 1) * NE] if isinstance(j, int) else tile_oh[:, bass.ds(j * NE, NE)]
                v.scalar_tensor_tensor(junk[u], xg[u][:, H:ROW], 1.0, one, ALU.mult, ALU.mult,
                                       accum_out=wcol[:, u:u + 1]).then_inc(r_w, 1)

            def weighted(j, u):
                dve.wait_ge(r_dn, j + 1)
                if not isinstance(j, int):
                    dve.wait_ge(added[u % 2], (j - u) * 8 + (16 * (u // 2) - 16))
                elif j >= RING:
                    dve.wait_ge(added[u % 2], 16 * (j // 2) - 16)
                dve.wait_ge(r_w, j + 1)
                v.tensor_copy(add_list[:, u:u + 1], column(j))
                v.tensor_scalar(y[:, u, :], ps_y[u % 2][:, 0:H], wcol[:, u:u + 1], None, ALU.mult).then_inc(r_y, 1)

            def step(j, u):
                dve.wait_ge(r_silu, j + 1)
                v.tensor_tensor(h[:, u % 2, :], ps_g[u % 2][:, I:GU], sg[:, u % 2, :], ALU.mult).then_inc(r_mul, 1)
                row_weight(j + 2, (u + 2) % RING, (j - u) * 4 + 16 * ((u + 2) // RING + 1))
                if not isinstance(j, int) or j >= 1:
                    weighted(j - 1, (u - 1) % RING)

            dve.wait_ge(zeroed, 16 * 7)
            dve.wait_ge(idx_ready, 1)
            dve.wait_ge(spill_ready, 1)
            row_weight(0, 0, 16)
            row_weight(1, 1, 16)
            for u in range(RING):
                step(u, u)
            with dve.Fori(1, QUADS) as i:
                for u in range(RING):
                    step(i * RING + u, u)
            n_pairs = v.value_load(pairs[0:1, 1:2], min_val=0, max_val=SPILL // 2)
            with dve.Fori(QUADS, 2 * QUADS) as i:
                for pair in range(2):
                    with dve.If(i * 2 + (pair - 2 * QUADS) < n_pairs):
                        for u in (2 * pair, 2 * pair + 1):
                            step(i * RING + u, u)
            last_tile = n_pairs * 2 + (NE - 1)
            odd = n_pairs & 1
            with dve.If(odd < 1):
                weighted(last_tile, RING - 1)
            with dve.Else():
                weighted(last_tile, 1)

            into = [xnT[:, :, :].rearrange("p c (k h) -> p (c k) h", h=H), xn[:, :, 0:H]]
            for q in range(4):
                dve.wait_ge(acc_in[q], 32)
                part = xres[:, 2 * q:2 * q + 2, :]
                link(v.tensor_tensor(part, into[0][:, 2 * q:2 * q + 2, :], part, ALU.add))
                v.tensor_tensor(part, into[1][:, 2 * q:2 * q + 2, :], part, ALU.add).then_inc(final, 1)


def kernel(x, ctx_512, L0_xattn_W_k, L0_xattn_b_k, L0_xattn_ln_gamma, L0_xattn_ln_beta, L0_ffn_router_w,
           L0_ffn_router_b, L0_ffn_gate_w, L0_ffn_up_w, L0_ffn_down_w, L0_ffn_shared_gate_w,
           L0_ffn_shared_up_w, L0_ffn_shared_down_w):
    import numpy as np
    from concourse import bacc
    from concourse.bass_utils import run_bass_kernel_spmd

    def all_experts(routed, shared):
        return np.concatenate([np.asarray(routed), np.asarray(shared)[None]], axis=0)

    gate_up = np.concatenate([all_experts(L0_ffn_gate_w, L0_ffn_shared_gate_w),
                              all_experts(L0_ffn_up_w, L0_ffn_shared_up_w)], axis=1)
    down = all_experts(L0_ffn_down_w, L0_ffn_shared_down_w)
    arrays = {
        "x": np.asarray(x).reshape(T, H),
        "ctxT": np.asarray(ctx_512).transpose(2, 0, 1).reshape(D, T),
        "wkT": np.asarray(L0_xattn_W_k).T,
        "bk": np.asarray(L0_xattn_b_k).reshape(1, D),
        "gamma": np.asarray(L0_xattn_ln_gamma).reshape(1, S),
        "beta": np.asarray(L0_xattn_ln_beta).reshape(1, S),
        "routerT": np.asarray(L0_ffn_router_w).T.reshape(HC, P, NE).transpose(1, 0, 2),
        "router_b": np.asarray(L0_ffn_router_b).reshape(1, NE),
        "w_gu": gate_up.reshape(NE + 1, GU, HC, P).transpose(3, 0, 2, 1).reshape(P, -1),
        "w_dn": down.reshape(NE + 1, H, 2, IH).transpose(3, 0, 2, 1).reshape(IH, -1),
    }
    arrays = {f"in_{n}": np.ascontiguousarray(a) for n, a in arrays.items()}
    nc = bacc.Bacc("TRN2", target_bir_lowering=False, num_devices=1)
    ins = [nc.dram_tensor(n, a.shape, mybir.dt.from_np(a.dtype), kind="ExternalInput").ap() for n, a in arrays.items()]
    out = nc.dram_tensor("out", (T, H), F32, kind="ExternalOutput").ap()
    build(nc, *ins, out)
    r = run_bass_kernel_spmd(nc, [arrays], core_ids=[0])
    return r.results[0]["out"].reshape(B, S, H)
```
